# Optimizing a Trainium2 kernel written in Bass

```python
import numpy as np
import jax
import jax.numpy as jnp

def _softmax(x, axis=-1):
    return jax.nn.softmax(x, axis=axis)
def _gelu(x):
    return jax.nn.gelu(x, approximate=True)
def _silu(x):
    return jax.nn.silu(x)
def _sigmoid(x):
    return jax.nn.sigmoid(x)
def _layernorm(x, axis=-1, eps=1e-5):
    m = jnp.mean(x, axis=axis, keepdims=True)
    v = jnp.var(x, axis=axis, keepdims=True)
    return (x - m) / jnp.sqrt(v + eps)
def _scatter_add(tgt, idx, src, axis=0):
    return tgt.at[idx].add(src)
def _segment_sum(src, seg, n):
    return jax.ops.segment_sum(src, seg, n)

kernel_name = 'mk_conv_preact_d1_conv_nchw128_6e3da5'

def setup_inputs(seed: int = 0):
    np.random.seed(seed)
    _w = jnp.asarray
    def _rec_inputs():
        import jax
        import jax.numpy as jnp
        _gk = jax.random.key(seed)
        x = 7.22e-05 + 1 * jax.random.normal(jax.random.fold_in(_gk, 1), (16, 128, 64, 64), jnp.float32)
        return x
    x = _rec_inputs()
    def _L0_conv_setup():
        import jax, jax.numpy as jnp
        import numpy as np
        from jax import lax
        HIDDEN = 128

        def skew(x):
            B, C, H, W = x.shape
            Ws = W + H - 1
            rows = jnp.arange(H)[:, None]
            cols = jnp.arange(Ws)[None, :]
            src = cols - rows
            valid = (src >= 0) & (src < W)
            idx = jnp.clip(src, 0, W - 1)[None, None]
            g = jnp.take_along_axis(x, jnp.broadcast_to(idx, (B, C, H, Ws)), axis=3)
            return jnp.where(valid[None, None], g, jnp.zeros((), x.dtype))

        def unskew(y, W):
            B, C, H, Ws = y.shape
            idx = (jnp.arange(W)[None, :] + jnp.arange(H)[:, None])[None, None]
            return jnp.take_along_axis(y, jnp.broadcast_to(idx, (B, C, H, W)), axis=3)
        key = jax.random.key(seed)
        k1, k2, k3 = jax.random.split(key, 3)
        C = HIDDEN
        x = jax.random.normal(k1, (16, C, 64, 64), dtype=jnp.float32)
        w_is = jax.random.normal(k2, (4 * C, C), dtype=jnp.float32) * (1.0 / np.sqrt(C))
        b_is = jnp.zeros((4 * C,), dtype=jnp.float32)
        w_ss = jax.random.normal(k3, (4 * C, C, 2), dtype=jnp.float32) * (1.0 / np.sqrt(2 * C))
        b_ss = jnp.zeros((4 * C,), dtype=jnp.float32)
        return {'x': x, 'w_is': w_is, 'b_is': b_is, 'w_ss': w_ss, 'b_ss': b_ss}
    _L0_conv_all = _L0_conv_setup()
    _L0_conv_in = {k: v for k, v in _L0_conv_all.items() if k in ('w_is', 'b_is', 'w_ss', 'b_ss', )}
    del _L0_conv_all

    return {
        "x": x,
        "L0_conv_w_is": _L0_conv_in["w_is"],
        "L0_conv_b_is": _L0_conv_in["b_is"],
        "L0_conv_w_ss": _L0_conv_in["w_ss"],
        "L0_conv_b_ss": _L0_conv_in["b_ss"],
    }

def reference(x, L0_conv_w_is, L0_conv_b_is, L0_conv_w_ss, L0_conv_b_ss):
    import jax
    import jax.numpy as jnp
    def _L0_conv_ref(x, w_is, b_is, w_ss, b_ss):
        import jax, jax.numpy as jnp
        import numpy as np
        from jax import lax
        HIDDEN = 128

        def skew(x):
            B, C, H, W = x.shape
            Ws = W + H - 1
            rows = jnp.arange(H)[:, None]
            cols = jnp.arange(Ws)[None, :]
            src = cols - rows
            valid = (src >= 0) & (src < W)
            idx = jnp.clip(src, 0, W - 1)[None, None]
            g = jnp.take_along_axis(x, jnp.broadcast_to(idx, (B, C, H, Ws)), axis=3)
            return jnp.where(valid[None, None], g, jnp.zeros((), x.dtype))

        def unskew(y, W):
            B, C, H, Ws = y.shape
            idx = (jnp.arange(W)[None, :] + jnp.arange(H)[:, None])[None, None]
            return jnp.take_along_axis(y, jnp.broadcast_to(idx, (B, C, H, W)), axis=3)
        B, C, H, W = x.shape
        xs = skew(x)
        i_s = jnp.einsum('oi,bihw->bohw', w_is, xs) + b_is[None, :, None, None]

        def step(carry, ist):
            h, c = carry
            h_shift = jnp.pad(h, ((0, 0), (0, 0), (1, 0)))[:, :, :-1]
            s_s = jnp.einsum('oi,bih->boh', w_ss[:, :, 0], h_shift) + jnp.einsum('oi,bih->boh', w_ss[:, :, 1], h) + b_ss[None, :, None]
            gates = ist + s_s
            ofi = jax.nn.sigmoid(gates[:, :3 * C])
            o, f, ig = (ofi[:, :C], ofi[:, C:2 * C], ofi[:, 2 * C:])
            g = jnp.tanh(gates[:, 3 * C:])
            c_new = f * c + ig * g
            h_new = o * jnp.tanh(c_new)
            return ((h_new, c_new), h_new)
        h0 = jnp.zeros((B, C, H), dtype=x.dtype)
        c0 = jnp.zeros((B, C, H), dtype=x.dtype)
        i_s_t = jnp.moveaxis(i_s, 3, 0)
        _, hs = lax.scan(step, (h0, c0), i_s_t)
        out = jnp.moveaxis(hs, 0, 3)
        return unskew(out, W)

    def _gn(v, G=32, eps=1e-5):
        B_, C_, H_, W_ = v.shape
        g = v.reshape(B_, G, C_ // G, H_, W_)
        m = jnp.mean(g, axis=(2, 3, 4), keepdims=True)
        s = jnp.var(g, axis=(2, 3, 4), keepdims=True)
        return ((g - m) / jnp.sqrt(s + eps)).reshape(v.shape)

    def _ln_c(v, eps=1e-6):
        m = jnp.mean(v, axis=1, keepdims=True)
        s = jnp.var(v, axis=1, keepdims=True)
        return (v - m) / jnp.sqrt(s + eps)

    def _ln_t(v, eps=1e-5):
        m = jnp.mean(v, axis=-1, keepdims=True)
        s = jnp.var(v, axis=-1, keepdims=True)
        return (v - m) / jnp.sqrt(s + eps)

    def _to_tokens(v):
        B_, C_, H_, W_ = v.shape
        return v.reshape(B_, C_, H_ * W_).transpose(0, 2, 1)
    def _from_tokens(t, like):
        B_, C_, H_, W_ = like.shape
        return t.transpose(0, 2, 1).reshape(B_, C_, H_, W_)

    x = x + _L0_conv_ref(_gn(x), L0_conv_w_is, L0_conv_b_is, L0_conv_w_ss, L0_conv_b_ss)
    return x


_drawn_inputs = setup_inputs


def setup_inputs(seed=0):
    import zlib

    import numpy as np

    out = dict(_drawn_inputs(seed))
    spreads = {'L0_conv_b_is': (0.0, 0.1), 'L0_conv_b_ss': (0.0, 0.1)}
    factors = {}
    for name, (base, spread) in spreads.items():
        noise = np.random.default_rng([zlib.crc32(name.encode()), seed]).standard_normal(out[name].shape)
        drawn = base * np.exp(spread * noise) if base else spread * noise
        out[name] = jnp.asarray(drawn.astype(out[name].dtype))
    for name, factor in factors.items():
        out[name] = (out[name] * factor).astype(out[name].dtype)
    return out
```

```python
from contextlib import ExitStack

import concourse.bass as bass
from concourse import mybir

P = 128
C = 128
H = W = 64
NB = 16
CH = 2
B = NB // CH
G = 4
Q = 4
STEPS = H + W - 1
GROUP = 4
GN_EPS = 1e-5
SUB = 512
XBUF = 3
HBUF = 2

F32 = mybir.dt.float32
F16 = mybir.dt.float16
I32 = mybir.dt.int32
ALU = mybir.AluOpType
ACT = mybir.ActivationFunctionType
AX_X = mybir.AxisListType.X


def plan_blocks():
    blocks = []
    t = 0
    while t < STEPS:
        if t < H:
            lo, hi = 0, min(t + Q, H - 1)
        else:
            lo, hi = t - (W - 1), H - 1
        blocks.append((t, min(Q, STEPS - t), lo, hi - lo + 1))
        t += Q
    return blocks


BLOCKS = plan_blocks()
NBLK = len(BLOCKS)
OFFSET = [0]
for _t, _n, _lo, _rows in BLOCKS:
    OFFSET.append(OFFSET[-1] + _n * B * _rows)
TOTAL = OFFSET[-1]
MAXBLK = Q * B * H


def diagonal_lstm_program(nc, x, x_diag, w_all, b_is, b_ss, ident16, group_mean, out_diag):
    with ExitStack() as ctx:
        def sb(name, shape, dt):
            return ctx.enter_context(nc.sbuf_tensor(name, shape, dt))

        def sem(name):
            return ctx.enter_context(nc.semaphore(name))

        banks = [[ctx.enter_context(nc.psum_tensor(f"gate_{c}_{g}", [P, 512], F32)) for g in range(G)]
                 for c in range(CH)]
        w_nat = sb("w_nat", [P, G, 3, C], F32)
        w_scaled = sb("w_scaled", [P, G, 3 * C], F32)
        w_split = sb("w_split", [P, 2, G, 3, C], F16)
        w_t = sb("w_t", [P, 2, G, 3, C], F16)
        ident = sb("ident", [P, P], F16)
        gmean = sb("gmean", [P, P], F32)
        bias_in = sb("bias_in", [P, 2, G], F32)
        bias = sb("bias", [P, G], F32)
        row_max = sb("row_max", [P, G], F32)
        row_exp = sb("row_exp", [P, G], I32)
        up = sb("up", [P, G], F32)
        down = sb("down", [P, G], F32)
        stage = sb("stage", [P, 2, H * W], F32)
        stats = sb("stats", [P, H * W // SUB, 6], F32)
        moments = sb("moments", [P, CH, B, 2], F32)
        dev = sb("dev", [P, CH, 6, B], F32)
        mean = sb("mean", [P, CH, B], F32)
        rstd = sb("rstd", [P, CH, B], F32)
        x_raw = sb("x_raw", [P, CH, XBUF, MAXBLK], F32)
        x_norm = sb("x_norm", [P, CH, MAXBLK], F32)
        x_hi = sb("x_hi", [P, CH, HBUF, MAXBLK], F16)
        x_lo = sb("x_lo", [P, CH, HBUF, MAXBLK], F16)
        h_hi = sb("h_hi", [P, CH, B, H + 1], F16)
        h_lo = sb("h_lo", [P, CH, B, H + 1], F16)
        cell = sb("cell", [P, CH, B, H], F32)
        h_out = sb("h_out", [P, CH, MAXBLK], F32)
        act_f = sb("act_f", [P, CH, B * H], F32)
        act_i = sb("act_i", [P, CH, B * H], F32)
        act_g = sb("act_g", [P, CH, B * H], F32)
        act_o = sb("act_o", [P, CH, B * H], F32)
        tanh_c = sb("tanh_c", [P, CH, B * H], F32)

        s_consts = sem("consts_loaded")
        s_weights = sem("weights_loaded")
        s_stage = [sem(f"stage_loaded_{j}") for j in range(2)]
        s_stage_read = sem("stage_read")
        s_setup = sem("vector_setup_done")
        s_wsplit = sem("weights_split")
        s_wtrans = sem("weights_transposed")
        s_wready = sem("weights_ready")
        s_gm_in = sem("moments_ready")
        s_gm_out = sem("group_moments_ready")
        s_var = sem("variance_ready")
        s_std = sem("std_ready")
        s_init = sem("state_zeroed")
        s_x = [[sem(f"x_loaded_{c}_{j}") for j in range(XBUF)] for c in range(CH)]
        s_store = [[sem(f"out_stored_{c}_{j}") for j in range(XBUF)] for c in range(CH)]
        s_norm_ts = sem("x_scaled")
        s_norm = [sem(f"x_normalised_{c}") for c in range(CH)]
        s_xhi = [sem(f"x_hi_ready_{c}") for c in range(CH)]
        s_xlo = [sem(f"x_lo_ready_{c}") for c in range(CH)]
        s_pre = [[sem(f"gate_sum_{g}_{c}") for g in "figo"] for c in range(CH)]
        s_act = [[sem(f"gate_{g}_{c}") for g in "figo"] for c in range(CH)]
        s_fc = [sem(f"fc_ig_{c}") for c in range(CH)]
        s_c = [sem(f"cell_ready_{c}") for c in range(CH)]
        s_tc = [sem(f"tanh_cell_{c}") for c in range(CH)]
        s_h = [sem(f"h_ready_{c}") for c in range(CH)]
        s_hhi = [sem(f"h_hi_ready_{c}") for c in range(CH)]
        s_hlo = [sem(f"h_lo_ready_{c}") for c in range(CH)]
        s_new = [sem(f"new_rows_set_{c}") for c in range(CH)]
        s_out = [sem(f"out_added_{c}") for c in range(CH)]

        def block_ap(buf, k):
            _, n, _, rows = BLOCKS[k]
            return buf[:, 0:n * B * rows].rearrange("p (s b r) -> p s b r", s=n, b=B)

        def step_cols(buf, rows, i):
            n = B * rows
            return buf[:, bass.ds(i * n, n)]

        block = ctx.enter_context(nc.Block())

        @block.sync
        def _(sp):
            sp.dma_start(w_nat[:], w_all).then_inc(s_weights, 16)
            sp.dma_start(bias_in[:, 0, :], b_is).then_inc(s_weights, 16)
            sp.dma_start(bias_in[:, 1, :], b_ss).then_inc(s_weights, 16)
            sp.dma_start(ident[:], ident16).then_inc(s_consts, 16)
            sp.dma_start(gmean[:], group_mean).then_inc(s_consts, 16)
            for m in range(NB):
                if m >= 2:
                    sp.wait_ge(s_stage_read, m - 1)
                sp.dma_start(stage[:, m % 2, :], x[m]).then_inc(s_stage[m % 2], 16)

            def load(c, k):
                n = OFFSET[k + 1] - OFFSET[k]
                j = k % XBUF
                if k >= XBUF:
                    sp.wait_ge(s_store[c][j], 16 * (k // XBUF))
                sp.dma_start(x_raw[:, c, j, 0:n], x_diag[c, :, OFFSET[k]:OFFSET[k + 1]]).then_inc(s_x[c][j], 16)

            def store(c, k):
                t0, n, _, _ = BLOCKS[k]
                sp.wait_ge(s_out[c], t0 + n)
                size = OFFSET[k + 1] - OFFSET[k]
                sp.dma_start(out_diag[c, :, OFFSET[k]:OFFSET[k + 1]],
                             x_raw[:, c, k % XBUF, 0:size]).then_inc(s_store[c][k % XBUF], 16)

            for k in range(XBUF - 1):
                for c in range(CH):
                    load(c, k)
            for k in range(NBLK):
                if k + XBUF - 1 < NBLK:
                    if k == 0:
                        for c in range(CH):
                            load(c, XBUF - 1)
                    else:
                        for c in range(CH):
                            store(c, k - 1)
                        for c in range(CH):
                            load(c, k + XBUF - 1)
                elif k > 0:
                    for c in range(CH):
                        store(c, k - 1)
            for c in range(CH):
                store(c, NBLK - 1)
            for c in range(CH):
                for j in range(XBUF):
                    sp.wait_ge(s_store[c][j], 16 * len(range(j, NBLK, XBUF)))

        @block.vector
        def _(dve):
            done = [0]

            def link(ins):
                done[0] += 1
                ins.then_inc(s_setup, 1)
                dve.wait_ge(s_setup, done[0])

            nc.vector.memset(h_hi[:], 0.0)
            nc.vector.memset(h_lo[:], 0.0)
            nc.vector.memset(cell[:], 0.0).then_inc(s_init, 1)

            dve.wait_ge(s_weights, 48)
            nc.vector.tensor_tensor(bias[:], bias_in[:, 0, :], bias_in[:, 1, :], ALU.add)
            link(nc.vector.tensor_reduce(row_max[:], w_nat[:].rearrange("p g s i -> p g (s i)"), AX_X, ALU.max,
                                         apply_absolute_value=True))
            link(nc.vector.tensor_scalar(row_max[:], row_max[:], 2.0 ** -110, None, ALU.max))
            link(nc.vector.tensor_scalar(row_exp[:], row_max[:].bitcast(I32), 0x7F800000, None, ALU.bitwise_and))
            link(nc.vector.tensor_scalar(up[:].bitcast(I32), row_exp[:], -1.0, float(267 << 23), ALU.mult, ALU.add))
            link(nc.vector.tensor_scalar(down[:].bitcast(I32), row_exp[:], float(13 << 23), None, ALU.subtract))
            for g in range(G):
                nc.vector.tensor_scalar(w_scaled[:, g, :], w_nat[:, g].rearrange("p s i -> p (s i)"),
                                        up[:, g:g + 1], None, ALU.mult)
                last = nc.vector.tensor_scalar(w_split[:, 0, g].rearrange("p s i -> p (s i)"),
                                               w_nat[:, g].rearrange("p s i -> p (s i)"),
                                               up[:, g:g + 1], None, ALU.mult)
            link(last)
            last = nc.vector.tensor_tensor(w_split[:, 1].rearrange("p g s i -> p (g s i)"),
                                           w_scaled[:].rearrange("p g n -> p (g n)"),
                                           w_split[:, 0].rearrange("p g s i -> p (g s i)"), ALU.subtract)
            last.then_inc(s_wsplit, 1)
            wt = w_t[:].rearrange("p l g s i -> p (l g s i)")
            dve.wait_ge(s_wtrans, 1)
            for n in range(3):
                last = nc.vector.tensor_copy(wt[:, 1024 * n:1024 * n + 1024], banks[0][n][:].bitcast(F16))
            last.then_inc(s_wready, 1)

            def image_stats(m):
                c, b = divmod(m, B)
                dve.wait_ge(s_stage[m % 2], 16 * (m // 2 + 1))
                for n in range(H * W // SUB):
                    last = nc.vector.bn_stats(stats[:, n, :], stage[:, m % 2, n * SUB:(n + 1) * SUB])
                last.then_inc(s_stage_read, 1)
                dve.wait_ge(s_stage_read, m + 1)
                link(nc.vector.bn_aggr(moments[:, c, b, :], stats[:].rearrange("p n k -> p (n k)")))

            def group_stats(c):
                d = dev[:, c]
                link(nc.vector.tensor_copy(d[:, 0, :], moments[:, c, :, 0]))
                nc.vector.tensor_copy(d[:, 1, :], moments[:, c, :, 1]).then_inc(s_gm_in, 1)
                dve.wait_ge(s_gm_out, 2 * c + 1)
                link(nc.vector.tensor_copy(mean[:, c, :], banks[c][3][:, 0:B]))
                link(nc.vector.tensor_tensor(d[:, 2, :], d[:, 0, :], mean[:, c, :], ALU.subtract))
                link(nc.vector.tensor_tensor(d[:, 2, :], d[:, 2, :], d[:, 2, :], ALU.mult))
                dve.wait_ge(s_gm_in, 2 * c + 1)
                nc.vector.tensor_tensor(d[:, 1, :], d[:, 1, :], d[:, 2, :], ALU.add).then_inc(s_gm_in, 1)
                dve.wait_ge(s_gm_out, 2 * c + 2)
                nc.vector.tensor_scalar(d[:, 3, :], banks[c][3][:, 16:16 + B], GN_EPS, None,
                                        ALU.add).then_inc(s_var, 1)
                dve.wait_ge(s_std, c + 1)
                link(nc.vector.reciprocal(d[:, 5, :], d[:, 4, :]))
                link(nc.vector.tensor_tensor(d[:, 4, :], d[:, 5, :], d[:, 5, :], ALU.mult))
                link(nc.vector.tensor_tensor(d[:, 4, :], d[:, 4, :], d[:, 3, :], ALU.mult))
                link(nc.vector.tensor_scalar(d[:, 4, :], d[:, 4, :], -0.5, 1.5, ALU.mult, ALU.add))
                link(nc.vector.tensor_tensor(rstd[:, c, :], d[:, 5, :], d[:, 4, :], ALU.mult))

            n_ts = [0]

            def normalise(c, k):
                t0, n, lo, rows = BLOCKS[k]
                dve.wait_ge(s_x[c][k % XBUF], 16 * (k // XBUF + 1))
                if k > 0:
                    n_prev = BLOCKS[k - 1][0] + BLOCKS[k - 1][1]
                    dve.wait_ge(s_xhi[c], n_prev)
                    dve.wait_ge(s_xlo[c], n_prev)
                src = block_ap(x_raw[:, c, k % XBUF], k)
                dst = block_ap(x_norm[:, c], k)
                for b in range(B):
                    last = nc.vector.tensor_scalar(dst[:, :, b, :], src[:, :, b, :], mean[:, c, b:b + 1],
                                                   rstd[:, c, b:b + 1], ALU.subtract, ALU.mult)
                left = [(s, t0 + s + 1) for s in range(n) if t0 < H and t0 + s + 1 < lo + rows]
                if left:
                    n_ts[0] += 1
                    last.then_inc(s_norm_ts, 1)
                    dve.wait_ge(s_norm_ts, n_ts[0])
                    for s, r in left:
                        last = nc.vector.memset(dst[:, s, :, r - lo:rows], 0.0)
                last.then_inc(s_norm[c], 1)

            def new_rows(c, k):
                if k == 0 or BLOCKS[k - 1][2] + BLOCKS[k - 1][3] >= H:
                    return
                t0, _, _, rows = BLOCKS[k]
                old = BLOCKS[k - 1][3]
                more = rows - old
                dve.wait_ge(s_hlo[c], t0)
                for buf, first in ((h_hi[:, c], 1), (h_lo[:, c], 1), (cell[:, c], 0)):
                    state = buf[:, :, first + old - 1:first + old]
                    last = nc.vector.tensor_copy(buf[:, :, first + old:first + rows],
                                                 state.to_broadcast([P, B, more]))
                last.then_inc(s_new[c], 1)

            def cell_update(c, k, i):
                t0, n, lo, rows = BLOCKS[k]
                cols = B * rows
                v = lambda buf: buf[:, c, 0:cols].rearrange("p (b r) -> p b r", b=B)
                cc = cell[:, c, :, lo:lo + rows]
                dve.wait_ge(s_act[c][0], i + t0 + 1)
                nc.vector.tensor_tensor(v(act_f), v(act_f), cc, ALU.mult)
                dve.wait_ge(s_act[c][2], i + t0 + 1)
                nc.vector.tensor_tensor(act_g[:, c, 0:cols], act_g[:, c, 0:cols], act_i[:, c, 0:cols],
                                        ALU.mult).then_inc(s_fc[c], 1)
                dve.wait_ge(s_fc[c], i + t0 + 1)
                nc.vector.tensor_tensor(cc, v(act_f), v(act_g), ALU.add).then_inc(s_c[c], 1)

            def hidden(c, k, i):
                t0, n, lo, rows = BLOCKS[k]
                cols = B * rows
                h_view = step_cols(h_out[:, c], rows, i)
                hv = h_view.rearrange("p (b r) -> p b r", b=B)
                if k > 0:
                    dve.wait_ge(s_out[c], t0)
                dve.wait_ge(s_tc[c], i + t0 + 1)
                nc.vector.tensor_tensor(h_view, act_o[:, c, 0:cols], tanh_c[:, c, 0:cols],
                                        ALU.mult).then_inc(s_h[c], 1)
                dve.wait_ge(s_h[c], i + t0 + 1)
                hi = h_hi[:, c, :, lo + 1:lo + 1 + rows]
                nc.vector.tensor_scalar(hi, hv, 1.0, None, ALU.mult).then_inc(s_hhi[c], 1)
                dve.wait_ge(s_hhi[c], i + t0 + 1)
                nc.vector.tensor_tensor(h_lo[:, c, :, lo + 1:lo + 1 + rows], hv, hi,
                                        ALU.subtract).then_inc(s_hlo[c], 1)

            for m in range(NB):
                image_stats(m)
                if m % B == B - 1:
                    group_stats(m // B)
            for c in range(CH):
                normalise(c, 0)
            for k in range(NBLK):
                for c in range(CH):
                    new_rows(c, k)
                if k + 1 < NBLK:
                    for c in range(CH):
                        normalise(c, k + 1)
                with dve.Fori(0, BLOCKS[k][1]) as i:
                    for c in range(CH):
                        cell_update(c, k, i)
                        hidden(c, k, i)

        @block.scalar
        def _(act):
            for c in range(CH):
                act.wait_ge(s_var, c + 1)
                nc.scalar.activation(dev[:, c, 4, :], dev[:, c, 3, :], ACT.Sqrt).then_inc(s_std, 1)

            def split_high(c, k, i):
                _, _, _, rows = BLOCKS[k]
                nc.scalar.copy(step_cols(x_hi[:, c, k % HBUF], rows, i),
                               step_cols(x_norm[:, c], rows, i)).then_inc(s_xhi[c], 1)

            def gates(c, k, i):
                t0, n, lo, rows = BLOCKS[k]
                cols = B * rows
                for g, (buf, func) in enumerate(((act_f, ACT.Sigmoid), (act_i, ACT.Sigmoid),
                                                 (act_g, ACT.Tanh), (act_o, ACT.Sigmoid))):
                    act.wait_ge(s_pre[c][g], i + t0 + 1)
                    nc.scalar.activation(buf[:, c, 0:cols], banks[c][g][:, 0:cols], func, bias=bias[:, g:g + 1],
                                         scale=down[:, g:g + 1]).then_inc(s_act[c][g], 1)

            def tanh_cell(c, k, i):
                t0, n, lo, rows = BLOCKS[k]
                act.wait_ge(s_c[c], i + t0 + 1)
                nc.scalar.activation(tanh_c[:, c, 0:B * rows].rearrange("p (b r) -> p b r", b=B),
                                     cell[:, c, :, lo:lo + rows], ACT.Tanh).then_inc(s_tc[c], 1)

            for c in range(CH):
                act.wait_ge(s_norm[c], 1)
                for i in range(BLOCKS[0][1]):
                    split_high(c, 0, i)
            for k in range(NBLK):
                nxt = k + 1 < NBLK
                if nxt:
                    for c in range(CH):
                        act.wait_ge(s_norm[c], k + 2)
                        if k > 0:
                            act.wait_ge(s_pre[c][3], BLOCKS[k][0])
                steps = BLOCKS[k][1]
                ahead = BLOCKS[k + 1][1] if nxt else 0
                with act.Fori(0, steps) as i:
                    for c in range(CH):
                        gates(c, k, i)
                        tanh_cell(c, k, i)
                        if ahead == steps:
                            split_high(c, k + 1, i)
                if nxt and ahead != steps:
                    for c in range(CH):
                        for i in range(ahead):
                            split_high(c, k + 1, i)

        @block.gpsimd
        def _(pool):
            def split_low(c, k, i, n_hi):
                _, _, _, rows = BLOCKS[k]
                pool.wait_ge(s_xhi[c], n_hi)
                nc.gpsimd.tensor_tensor(step_cols(x_lo[:, c, k % HBUF], rows, i), step_cols(x_norm[:, c], rows, i),
                                        step_cols(x_hi[:, c, k % HBUF], rows, i), ALU.subtract).then_inc(s_xlo[c], 1)

            def add_x(c, k, i):
                t0, _, _, rows = BLOCKS[k]
                pool.wait_ge(s_h[c], i + t0 + 1)
                here = step_cols(x_raw[:, c, k % XBUF], rows, i)
                nc.gpsimd.tensor_tensor(here, here, step_cols(h_out[:, c], rows, i), ALU.add).then_inc(s_out[c], 1)

            for c in range(CH):
                for i in range(BLOCKS[0][1]):
                    split_low(c, 0, i, i + 1)
            for k in range(NBLK):
                nxt = k + 1 < NBLK
                steps = BLOCKS[k][1]
                ahead = BLOCKS[k + 1][1] if nxt else 0
                if nxt:
                    for c in range(CH):
                        pool.wait_ge(s_norm[c], k + 2)
                with pool.Fori(0, steps) as i:
                    for c in range(CH):
                        add_x(c, k, i)
                        if ahead == steps:
                            split_low(c, k + 1, i, i + BLOCKS[k + 1][0] + 1)
                if nxt and ahead != steps:
                    for c in range(CH):
                        for i in range(ahead):
                            split_low(c, k + 1, i, i + BLOCKS[k + 1][0] + 1)

        @block.tensor
        def _(pe):
            pe.wait_ge(s_consts, 32)
            pe.wait_ge(s_wsplit, 1)
            n = 0
            for l in range(2):
                for g in range(G):
                    for s in range(3):
                        dst = banks[0][n // 8][:].bitcast(F16)[:, (n % 8) * C:(n % 8 + 1) * C]
                        last = nc.tensor.transpose(dst, w_split[:, l, g, s, :], ident[:])
                        n += 1
            last.then_inc(s_wtrans, 1)
            for c in range(CH):
                for v, col in ((0, 0), (1, 16)):
                    pe.wait_ge(s_gm_in, 2 * c + v + 1)
                    nc.tensor.matmul(banks[c][3][:, col:col + B], gmean[:], dev[:, c, v, :],
                                     start=True, stop=True).then_inc(s_gm_out, 1)
            pe.wait_ge(s_wready, 1)
            pe.wait_ge(s_var, CH)
            pe.wait_ge(s_init, 1)

            IS, SHIFT, OWN = 0, 1, 2

            def input_products(c, k, i):
                t0, n, lo, rows = BLOCKS[k]
                cols = B * rows
                hi = step_cols(x_hi[:, c, k % HBUF], rows, i)
                low = step_cols(x_lo[:, c, k % HBUF], rows, i)
                for g in range(G):
                    dst = banks[c][g][:, 0:cols]
                    nc.tensor.matmul(dst, w_t[:, 0, g, IS, :], hi, start=True, stop=False)
                    nc.tensor.matmul(dst, w_t[:, 1, g, IS, :], hi, start=False, stop=False)
                    nc.tensor.matmul(dst, w_t[:, 0, g, IS, :], low, start=False, stop=False)

            def state_products(c, k):
                t0, n, lo, rows = BLOCKS[k]
                cols = B * rows
                views = {}
                for part, first in ((SHIFT, lo), (OWN, lo + 1)):
                    views[part] = (h_hi[:, c, :, first:first + rows], h_lo[:, c, :, first:first + rows])
                for g in range(G):
                    dst = banks[c][g][:, 0:cols].rearrange("p (b r) -> p b r", b=B)
                    for part in (SHIFT, OWN):
                        hi, low = views[part]
                        nc.tensor.matmul(dst, w_t[:, 0, g, part, :], hi, start=False, stop=False)
                        nc.tensor.matmul(dst, w_t[:, 1, g, part, :], hi, start=False, stop=False)
                        last = nc.tensor.matmul(dst, w_t[:, 0, g, part, :], low, start=False, stop=part == OWN)
                    last.then_inc(s_pre[c][g], 1)

            made = [0] * CH
            for k in range(NBLK):
                t0, n, lo, rows = BLOCKS[k]
                for c in range(CH):
                    pe.wait_ge(s_xlo[c], t0 + n)
                    if k > 0 and BLOCKS[k - 1][2] + BLOCKS[k - 1][3] < H:
                        made[c] += 1
                        pe.wait_ge(s_new[c], made[c])
                if k == 0:
                    first, start = 1, 1
                    for c in range(CH):
                        input_products(c, k, 0)
                        state_products(c, k)
                else:
                    first = 0
                with pe.Fori(first, n) as i:
                    for c in range(CH):
                        pe.wait_ge(s_act[c][3], i + t0)
                        input_products(c, k, i)
                        pe.wait_ge(s_hlo[c], i + t0)
                        state_products(c, k)


def _diagonal_index():
    import numpy as np
    image, row, col = [], [], []
    for t0, n, lo, rows in BLOCKS:
        t, b, r = np.meshgrid(np.arange(t0, t0 + n), np.arange(B), np.arange(lo, lo + rows), indexing="ij")
        image.append(b.ravel())
        row.append(r.ravel())
        col.append((t - r).ravel())
    image, row, col = (np.concatenate(a) for a in (image, row, col))
    return image, row, col, (col >= 0) & (col < W)


def kernel(x, L0_conv_w_is, L0_conv_b_is, L0_conv_w_ss, L0_conv_b_ss):
    import numpy as np
    import concourse.bacc as bacc
    from concourse.bass_utils import run_bass_kernel_spmd

    x = np.asarray(x)
    w_is, b_is, w_ss, b_ss = (np.asarray(a) for a in (L0_conv_w_is, L0_conv_b_is, L0_conv_w_ss, L0_conv_b_ss))
    order = [1, 2, 3, 0]
    parts = np.stack([w_is, w_ss[:, :, 0], w_ss[:, :, 1]], axis=1)
    w_all = parts.reshape(G, C, 3, C)[order].transpose(1, 0, 2, 3)

    image, row, col, pixel = _diagonal_index()
    chains = x.reshape(CH, B, C, H, W)
    x_diag = np.zeros((CH, C, TOTAL), x.dtype)
    for c in range(CH):
        x_diag[c][:, pixel] = chains[c][image[pixel], :, row[pixel], col[pixel]].T

    arrays = {
        "x": np.ascontiguousarray(x.reshape(NB, C, H * W)),
        "x_diag": x_diag,
        "w_all": np.ascontiguousarray(w_all),
        "b_is": np.ascontiguousarray(b_is.reshape(G, C)[order].T),
        "b_ss": np.ascontiguousarray(b_ss.reshape(G, C)[order].T),
        "ident16": np.eye(P, dtype=np.float16),
        "group_mean": np.kron(np.eye(C // GROUP), np.full((GROUP, GROUP), 1.0 / GROUP)).astype(np.float32),
    }
    nc = bacc.Bacc("TRN2", target_bir_lowering=False, num_devices=1)
    args = [nc.dram_tensor(f"in_{n}", a.shape, mybir.dt.from_np(a.dtype), kind="ExternalInput").ap()
            for n, a in arrays.items()]
    args.append(nc.dram_tensor("out_diag", (CH, C, TOTAL), F32, kind="ExternalOutput").ap())
    diagonal_lstm_program(nc, *args)
    result = run_bass_kernel_spmd(nc, [{f"in_{n}": a for n, a in arrays.items()}], core_ids=[0])
    got = result.results[0]["out_diag"]
    out = np.empty((CH, B, C, H, W), got.dtype)
    for c in range(CH):
        out[c][image[pixel], :, row[pixel], col[pixel]] = got[c][:, pixel].T
    return out.reshape(NB, C, H, W)
```

```python
from contextlib import ExitStack

import concourse.bass as bass
from concourse import mybir

P = 128
C = 128
H = W = 64
NB = 16
CH = 2
B = NB // CH
G = 4
Q = 4
STEPS = H + W - 1
GROUP = 4
GN_EPS = 1e-5
SUB = 512
LAG = 5
LOOP_ROWS = 60
STAGES = 3
XBUF = 3
HBUF = 2

F32 = mybir.dt.float32
F16 = mybir.dt.float16
I32 = mybir.dt.int32
ALU = mybir.AluOpType
ACT = mybir.ActivationFunctionType
AX_X = mybir.AxisListType.X


def plan_blocks():
    blocks, t = [], 0
    while t < STEPS:
        n = Q if t else Q - 1
        lo = max(0, t - (W - 1))
        hi = min(t + n, H - 1)
        blocks.append((t, n, lo, hi - lo + 1))
        t += n
    return blocks


BLOCKS = plan_blocks()
NBLK = len(BLOCKS)
CHUNKS = H * W // SUB
ROUNDS = [[(c, r - lag) for c, lag in ((0, 0), (1, LAG)) if 0 <= r - lag < NBLK] for r in range(NBLK + LAG)]


def looped(r):
    return len(ROUNDS[r]) == CH and sum(BLOCKS[k][3] for _, k in ROUNDS[r]) >= LOOP_ROWS and not uneven(r)


def uneven(r):
    return len({BLOCKS[k][1] for _, k in ROUNDS[r]}) > 1


def round_steps(r):
    most = max(BLOCKS[k][1] for _, k in ROUNDS[r])
    return [(i - (most - BLOCKS[k][1]), c, k) for i in range(most) for c, k in ROUNDS[r]
            if i >= most - BLOCKS[k][1]]


def run_round(engine, r, step):
    if looped(r):
        with engine.Fori(0, BLOCKS[ROUNDS[r][0][1]][1]) as i:
            for c, k in ROUNDS[r]:
                step(c, k, i)
    else:
        for i, c, k in round_steps(r):
            step(c, k, i)


def has_left(k):
    t0, n, lo, rows = BLOCKS[k]
    return t0 + n == lo + rows - 1


def brings_rows(k):
    return 0 < k < NBLK and BLOCKS[k][2] + BLOCKS[k][3] > BLOCKS[k - 1][2] + BLOCKS[k - 1][3]


def share(k, i):
    n = BLOCKS[k][1]
    if n * (B // n) == B:
        return i * (B // n), B // n
    return i * -(-B // n), min(-(-B // n), B - i * -(-B // n))


def stats_plan():
    steps = sum(BLOCKS[r][1] for r in range(LAG))
    total = B * CHUNKS
    return [total * (n + 1) // steps - total * n // steps for n in range(steps)]


STATS_PLAN = stats_plan()


OFFSET = [0]
for _t, _n, _lo, _rows in BLOCKS:
    OFFSET.append(OFFSET[-1] + _n * B * _rows)
TOTAL = OFFSET[-1]
MAXBLK = Q * B * H


def diagonal_lstm_program(nc, x, x_diag, w_all, b_is, b_ss, ident16, group_mean, out_diag):
    with ExitStack() as ctx:
        def sb(name, shape, dt):
            return ctx.enter_context(nc.sbuf_tensor(name, shape, dt))

        def sem(name):
            return ctx.enter_context(nc.semaphore(name))

        banks = [[ctx.enter_context(nc.psum_tensor(f"gate_{c}_{g}", [P, 512], F32)) for g in range(G)]
                 for c in range(CH)]
        w_nat = sb("w_nat", [P, G, 3, C], F32)
        w_split = sb("w_split", [P, 2, G, 3, C], F16)
        w_t = sb("w_t", [P, 2, G, 3, C], F16)
        ident = sb("ident", [P, P], F16)
        gmean = sb("gmean", [P, P], F32)
        bias_in = sb("bias_in", [P, 2, G], F32)
        bias = sb("bias", [P, G], F32)
        row_max = sb("row_max", [P, G], F32)
        row_exp = sb("row_exp", [P, G], I32)
        up = sb("up", [P, G], F32)
        down = sb("down", [P, G], F32)
        stage = sb("stage", [P, STAGES, H * W], F32)
        stats = sb("stats", [P, H * W // SUB, 6], F32)
        mask = sb("mask", [P, Q, Q], F32)
        half = sb("half", [P, B], F32)
        moments = sb("moments", [P, CH, B, 2], F32)
        dev = sb("dev", [P, CH, 6, B], F32)
        mean = sb("mean", [P, CH, B], F32)
        rstd = sb("rstd", [P, CH, B], F32)
        x_raw = sb("x_raw", [P, CH, XBUF, MAXBLK], F32)
        x_norm = sb("x_norm", [P, CH, MAXBLK], F32)
        x_hi = sb("x_hi", [P, CH, HBUF, MAXBLK], F16)
        x_lo = sb("x_lo", [P, CH, HBUF, MAXBLK], F16)
        h_hi = sb("h_hi", [P, CH, B, H + 1], F16)
        h_lo = sb("h_lo", [P, CH, B, H + 1], F16)
        cell = sb("cell", [P, CH, B, H], F32)
        h_out = sb("h_out", [P, CH, MAXBLK], F32)
        act_f = sb("act_f", [P, CH, B * H], F32)
        act_i = sb("act_i", [P, CH, B * H], F32)
        act_g = sb("act_g", [P, CH, B * H], F32)
        act_o = sb("act_o", [P, CH, B * H], F32)
        tanh_c = act_i

        s_consts = sem("consts_loaded")
        s_weights = sem("weights_loaded")
        s_stage = [sem(f"stage_loaded_{j}") for j in range(STAGES)]
        s_stage_read = sem("stage_chunks_read")
        s_setup = sem("vector_setup_done")
        s_wsplit = sem("weights_split")
        s_wtrans = sem("weights_transposed")
        s_wready = sem("weights_ready")
        s_gm_in = sem("moments_ready")
        s_gm_out = sem("group_moments_ready")
        s_var = sem("variance_ready")
        s_rstd = sem("rstd_ready")
        s_init = sem("state_zeroed")
        s_x = [[sem(f"x_loaded_{c}_{j}") for j in range(XBUF)] for c in range(CH)]
        s_store = [[sem(f"out_stored_{c}_{j}") for j in range(XBUF)] for c in range(CH)]
        s_scaled = [sem(f"x_scaled_{c}") for c in range(CH)]
        s_norm = [sem(f"x_normalised_{c}") for c in range(CH)]
        s_xhi = [sem(f"x_hi_ready_{c}") for c in range(CH)]
        s_xlo = [sem(f"x_lo_ready_{c}") for c in range(CH)]
        s_pre = [[sem(f"gate_sum_{g}_{c}") for g in "figo"] for c in range(CH)]
        s_act = [[sem(f"gate_{g}_{c}") for g in "figo"] for c in range(CH)]
        s_fc = [sem(f"fc_ig_{c}") for c in range(CH)]
        s_c = [sem(f"cell_ready_{c}") for c in range(CH)]
        s_tc = [sem(f"tanh_cell_{c}") for c in range(CH)]
        s_h = [sem(f"h_ready_{c}") for c in range(CH)]
        s_hhi = [sem(f"h_hi_ready_{c}") for c in range(CH)]
        s_hlo = [sem(f"h_lo_ready_{c}") for c in range(CH)]
        s_new = [sem(f"new_rows_set_{c}") for c in range(CH)]
        s_out = [sem(f"out_added_{c}") for c in range(CH)]

        def block_ap(buf, k):
            _, n, _, rows = BLOCKS[k]
            return buf[:, 0:n * B * rows].rearrange("p (s b r) -> p s b r", s=n, b=B)

        def step_cols(buf, rows, i):
            n = B * rows
            return buf[:, bass.ds(i * n, n)]

        images_by_round, loaded = [], B
        for r in range(LAG):
            read = sum(STATS_PLAN[:BLOCKS[r][0]]) // CHUNKS
            upto = min(B + read + STAGES, NB)
            images_by_round.append(range(loaded, upto))
            loaded = upto
        assert loaded == NB

        block = ctx.enter_context(nc.Block())

        @block.sync
        def _(sp):
            sp.dma_start(w_nat[:], w_all).then_inc(s_weights, 16)
            sp.dma_start(bias_in[:, 0, :], b_is).then_inc(s_weights, 16)
            sp.dma_start(bias_in[:, 1, :], b_ss).then_inc(s_weights, 16)
            sp.dma_start(ident[:], ident16).then_inc(s_consts, 16)
            sp.dma_start(gmean[:], group_mean).then_inc(s_consts, 16)
            def load_image(m):
                if m >= STAGES:
                    sp.wait_ge(s_stage_read, CHUNKS * (m - STAGES + 1))
                sp.dma_start(stage[:, m % STAGES, :], x[m]).then_inc(s_stage[m % STAGES], 16)

            def load(c, k):
                n = OFFSET[k + 1] - OFFSET[k]
                j = k % XBUF
                if k >= XBUF:
                    sp.wait_ge(s_store[c][j], 16 * (k // XBUF))
                sp.dma_start(x_raw[:, c, j, 0:n], x_diag[c, :, OFFSET[k]:OFFSET[k + 1]]).then_inc(s_x[c][j], 16)

            def store(c, k):
                t0, n, _, _ = BLOCKS[k]
                sp.wait_ge(s_out[c], t0 + n)
                size = OFFSET[k + 1] - OFFSET[k]
                sp.dma_start(out_diag[c, :, OFFSET[k]:OFFSET[k + 1]],
                             x_raw[:, c, k % XBUF, 0:size]).then_inc(s_store[c][k % XBUF], 16)

            for m in range(B):
                load_image(m)
                if m == B // 2:
                    for k in range(XBUF):
                        load(0, k)
            for r, pairs in enumerate(ROUNDS):
                for c, k in pairs:
                    if k > 0:
                        store(c, k - 1)
                        if k + XBUF - 1 < NBLK:
                            load(c, k + XBUF - 1)
                if r < LAG:
                    for m in images_by_round[r]:
                        load_image(m)
                if r == LAG - 1:
                    for k in range(XBUF):
                        load(1, k)
            for c in range(CH):
                store(c, NBLK - 1)
            for c in range(CH):
                for j in range(XBUF):
                    sp.wait_ge(s_store[c][j], 16 * len(range(j, NBLK, XBUF)))

        @block.vector
        def _(dve):
            done = [0]

            def link(ins):
                done[0] += 1
                ins.then_inc(s_setup, 1)
                dve.wait_ge(s_setup, done[0])

            nc.vector.memset(half[:], -0.5)
            link(nc.vector.memset(mask[:], 0.0))
            for s in range(1, Q):
                nc.vector.memset(mask[:, s, 0:s], 1.0)
            nc.vector.memset(h_hi[:], 0.0)
            nc.vector.memset(h_lo[:], 0.0)
            nc.vector.memset(cell[:], 0.0).then_inc(s_init, 1)

            dve.wait_ge(s_weights, 48)
            nc.vector.tensor_tensor(bias[:], bias_in[:, 0, :], bias_in[:, 1, :], ALU.add)
            link(nc.vector.tensor_reduce(row_max[:], w_nat[:].rearrange("p g s i -> p g (s i)"), AX_X, ALU.max,
                                         apply_absolute_value=True))
            link(nc.vector.tensor_scalar(row_max[:], row_max[:], 2.0 ** -110, None, ALU.max))
            link(nc.vector.tensor_scalar(row_exp[:], row_max[:].bitcast(I32), 0x7F800000, None, ALU.bitwise_and))
            link(nc.vector.tensor_scalar(up[:].bitcast(I32), row_exp[:], -1.0, float(267 << 23), ALU.mult, ALU.add))
            link(nc.vector.tensor_scalar(down[:].bitcast(I32), row_exp[:], float(13 << 23), None, ALU.subtract))
            for g in range(G):
                last = nc.vector.tensor_scalar(w_split[:, 0, g].rearrange("p s i -> p (s i)"),
                                               w_nat[:, g].rearrange("p s i -> p (s i)"),
                                               up[:, g:g + 1], None, ALU.mult)
            link(last)
            for g in range(G):
                flat = w_nat[:, g].rearrange("p s i -> p (s i)")
                last = nc.vector.tensor_scalar(flat, flat, up[:, g:g + 1], None, ALU.mult)
            link(last)
            last = nc.vector.tensor_tensor(w_split[:, 1].rearrange("p g s i -> p (g s i)"),
                                           w_nat[:].rearrange("p g s i -> p (g s i)"),
                                           w_split[:, 0].rearrange("p g s i -> p (g s i)"), ALU.subtract)
            last.then_inc(s_wsplit, 1)
            wt = w_t[:].rearrange("p l g s i -> p (l g s i)")
            dve.wait_ge(s_wtrans, 1)
            for n in range(3):
                last = nc.vector.tensor_copy(wt[:, 1024 * n:1024 * n + 1024], banks[0][n][:].bitcast(F16))
            last.then_inc(s_wready, 1)

            def chunk_stats(n):
                m, part = divmod(n, CHUNKS)
                if part == 0:
                    dve.wait_ge(s_stage[m % STAGES], 16 * (m // STAGES + 1))
                    if m:
                        dve.wait_ge(s_setup, done[0])
                nc.vector.bn_stats(stats[:, part, :],
                                   stage[:, m % STAGES, part * SUB:(part + 1) * SUB]).then_inc(s_stage_read, 1)
                if part == CHUNKS - 1:
                    dve.wait_ge(s_stage_read, CHUNKS * (m + 1))
                    done[0] += 1
                    nc.vector.bn_aggr(moments[:, m // B, m % B, :],
                                      stats[:].rearrange("p n k -> p (n k)")).then_inc(s_setup, 1)

            def group_stats(c):
                d = dev[:, c]
                dve.wait_ge(s_setup, done[0])
                link(nc.vector.tensor_copy(d[:, 0, :], moments[:, c, :, 0]))
                nc.vector.tensor_copy(d[:, 1, :], moments[:, c, :, 1]).then_inc(s_gm_in, 1)
                dve.wait_ge(s_gm_out, 2 * c + 1)
                link(nc.vector.tensor_copy(mean[:, c, :], banks[c][3][:, 0:B]))
                link(nc.vector.tensor_tensor(d[:, 2, :], d[:, 0, :], mean[:, c, :], ALU.subtract))
                link(nc.vector.tensor_tensor(d[:, 2, :], d[:, 2, :], d[:, 2, :], ALU.mult))
                dve.wait_ge(s_gm_in, 2 * c + 1)
                nc.vector.tensor_tensor(d[:, 1, :], d[:, 1, :], d[:, 2, :], ALU.add).then_inc(s_gm_in, 1)
                dve.wait_ge(s_gm_out, 2 * c + 2)
                nc.vector.tensor_scalar(d[:, 3, :], banks[c][3][:, 16:16 + B], GN_EPS, None,
                                        ALU.add).then_inc(s_var, 1)
                dve.wait_ge(s_rstd, c + 1)
                link(nc.vector.tensor_tensor(d[:, 4, :], d[:, 5, :], d[:, 5, :], ALU.mult))
                link(nc.vector.tensor_tensor(d[:, 4, :], d[:, 4, :], d[:, 3, :], ALU.mult))
                link(nc.vector.tensor_scalar(d[:, 4, :], d[:, 4, :], -0.5, 1.5, ALU.mult, ALU.add))
                link(nc.vector.tensor_tensor(rstd[:, c, :], d[:, 5, :], d[:, 4, :], ALU.mult))

            def normalise(c, k, first, count, n):
                src = block_ap(x_raw[:, c, k % XBUF], k)
                dst = block_ap(x_norm[:, c], k)
                for j in range(count):
                    last = nc.vector.tensor_scalar(dst[:, :, bass.ds(first + j, 1), :], src[:, :, bass.ds(first + j, 1), :],
                                                   mean[:, c, bass.ds(first + j, 1)],
                                                   rstd[:, c, bass.ds(first + j, 1)], ALU.subtract, ALU.mult)
                if not has_left(k):
                    last.then_inc(s_norm[c], 1)
                    return
                last.then_inc(s_scaled[c], 1)
                dve.wait_ge(s_scaled[c], n)
                _, steps, _, rows = BLOCKS[k]
                new = dst[:, :, bass.ds(first, count), rows - steps:rows]
                keep = mask[:, 0:steps, 0:steps].unsqueeze(2).to_broadcast([P, steps, count, steps])
                nc.vector.tensor_tensor(new, new, keep, ALU.mult).then_inc(s_norm[c], 1)

            def block_arrived(c, k):
                dve.wait_ge(s_x[c][k % XBUF], 16 * (k // XBUF + 1))
                if k > 0:
                    dve.wait_ge(s_xlo[c], 1 + BLOCKS[k - 1][0])

            def cell_update(c, k, i):
                t0, n, lo, rows = BLOCKS[k]
                cols = B * rows
                v = lambda buf: buf[:, c, 0:cols].rearrange("p (b r) -> p b r", b=B)
                cc = cell[:, c, :, lo:lo + rows]
                if brings_rows(k) and (not isinstance(i, int) or i == 0):
                    dve.wait_ge(s_new[c], t0)
                dve.wait_ge(s_act[c][0], i + t0 + 1)
                nc.vector.tensor_tensor(v(act_f), v(act_f), cc, ALU.mult)
                dve.wait_ge(s_act[c][2], i + t0 + 1)
                nc.vector.tensor_tensor(act_g[:, c, 0:cols], act_g[:, c, 0:cols], act_i[:, c, 0:cols],
                                        ALU.mult).then_inc(s_fc[c], 1)
                dve.wait_ge(s_fc[c], i + t0 + 1)
                if brings_rows(k + 1) and not isinstance(i, int):
                    dve.wait_ge(s_new[c], i + t0)
                nc.vector.tensor_tensor(cc, v(act_f), v(act_g), ALU.add).then_inc(s_c[c], 1)

            def hidden(c, k, i):
                t0, n, lo, rows = BLOCKS[k]
                cols = B * rows
                h_view = step_cols(h_out[:, c], rows, i)
                hv = h_view.rearrange("p (b r) -> p b r", b=B)
                if k > 0:
                    dve.wait_ge(s_out[c], t0)
                dve.wait_ge(s_tc[c], i + t0 + 1)
                hi = h_hi[:, c, :, lo + 1:lo + 1 + rows]
                v = lambda buf: buf[:, c, 0:cols].rearrange("p (b r) -> p b r", b=B)
                nc.vector.tensor_tensor(hi, v(act_o), v(tanh_c), ALU.mult).then_inc(s_hhi[c], 1)
                nc.vector.tensor_tensor(h_view, act_o[:, c, 0:cols], tanh_c[:, c, 0:cols],
                                        ALU.mult).then_inc(s_h[c], 1)
                dve.wait_ge(s_h[c], i + t0 + 1)
                nc.vector.tensor_tensor(h_lo[:, c, :, lo + 1:lo + 1 + rows], hv, hi,
                                        ALU.subtract).then_inc(s_hlo[c], 1)

            def step(c, k, i):
                if k + 1 < NBLK:
                    if not isinstance(i, int) or i == 0:
                        block_arrived(c, k + 1)
                    normalise(c, k + 1, *share(k, i), i + BLOCKS[k][0] + 2)
                cell_update(c, k, i)
                hidden(c, k, i)

            for n in range(B * CHUNKS):
                chunk_stats(n)
            group_stats(0)
            block_arrived(0, 0)
            normalise(0, 0, 0, B, 1)
            for r, pairs in enumerate(ROUNDS):
                if r < LAG:
                    k = r
                    for i in range(BLOCKS[k][1]):
                        at = BLOCKS[k][0] + i
                        first = B * CHUNKS + sum(STATS_PLAN[:at])
                        early = (STATS_PLAN[at] + 1) // 2
                        for n in range(first, first + early):
                            chunk_stats(n)
                        if i == 0:
                            block_arrived(0, k + 1)
                        normalise(0, k + 1, *share(k, i), i + BLOCKS[k][0] + 2)
                        cell_update(0, k, i)
                        for n in range(first + early, first + STATS_PLAN[at]):
                            chunk_stats(n)
                        hidden(0, k, i)
                else:
                    run_round(dve, r, step)
                if r == LAG - 1:
                    group_stats(1)
                    block_arrived(1, 0)
                    normalise(1, 0, 0, B, 1)

        @block.scalar
        def _(act):
            def split_high(c, k, first, count, n):
                act.wait_ge(s_norm[c], n)
                part = (slice(None), slice(None), bass.ds(first, count))
                nc.scalar.copy(block_ap(x_hi[:, c, k % HBUF], k)[part],
                               block_ap(x_norm[:, c], k)[part]).then_inc(s_xhi[c], 1)

            def gates(c, k, i):
                t0, n, lo, rows = BLOCKS[k]
                cols = B * rows
                for g, (buf, func) in enumerate(((act_f, ACT.Sigmoid), (act_i, ACT.Sigmoid),
                                                 (act_g, ACT.Tanh), (act_o, ACT.Sigmoid))):
                    act.wait_ge(s_pre[c][g], i + t0 + 1)
                    nc.scalar.activation(buf[:, c, 0:cols], banks[c][g][:, 0:cols], func, bias=bias[:, g:g + 1],
                                         scale=down[:, g:g + 1]).then_inc(s_act[c][g], 1)

            def tanh_cell(c, k, i):
                t0, n, lo, rows = BLOCKS[k]
                act.wait_ge(s_c[c], i + t0 + 1)
                nc.scalar.activation(tanh_c[:, c, 0:B * rows].rearrange("p (b r) -> p b r", b=B),
                                     cell[:, c, :, lo:lo + rows], ACT.Tanh).then_inc(s_tc[c], 1)

            def step(c, k, i):
                gates(c, k, i)
                if k + 1 < NBLK:
                    split_high(c, k + 1, *share(k, i), i + BLOCKS[k][0] + 2)
                tanh_cell(c, k, i)

            for r, pairs in enumerate(ROUNDS):
                for c, k in pairs:
                    if k == 0:
                        split_high(c, 0, 0, B, 1)
                    elif k + 1 < NBLK:
                        act.wait_ge(s_pre[c][3], BLOCKS[k][0])
                run_round(act, r, step)

        @block.gpsimd
        def _(pool):
            def split_low(c, k, first, count, n):
                pool.wait_ge(s_xhi[c], n)
                part = (slice(None), slice(None), bass.ds(first, count))
                nc.gpsimd.tensor_tensor(block_ap(x_lo[:, c, k % HBUF], k)[part], block_ap(x_norm[:, c], k)[part],
                                        block_ap(x_hi[:, c, k % HBUF], k)[part],
                                        ALU.subtract).then_inc(s_xlo[c], 1)

            def new_rows(c, k, i):
                t0, _, _, rows = BLOCKS[k]
                if not brings_rows(k + 1) or (isinstance(i, int) and i < BLOCKS[k][1] - 1):
                    return
                more = BLOCKS[k + 1][3] - rows
                pool.wait_ge(s_hlo[c], i + t0 + 1)
                new = [P, B, more]
                rest = bass.ds(rows + 1, more)
                nc.gpsimd.tensor_tensor(h_lo[:, c, :, rest], h_lo[:, c, :, rows:rows + 1].to_broadcast(new),
                                        h_lo[:, c, :, 0:1].to_broadcast(new), ALU.add)
                for buf, first in ((h_hi[:, c], 1), (cell[:, c], 0)):
                    state = buf[:, :, first + rows - 1:first + rows]
                    last = nc.gpsimd.tensor_copy(buf[:, :, first + rows:first + rows + more],
                                                 state.to_broadcast([P, B, more]))
                last.then_inc(s_new[c], BLOCKS[k][1] if isinstance(i, int) else 1)

            def add_x(c, k, i):
                t0, _, _, rows = BLOCKS[k]
                pool.wait_ge(s_h[c], i + t0 + 1)
                here = step_cols(x_raw[:, c, k % XBUF], rows, i)
                nc.gpsimd.tensor_tensor(here, here, step_cols(h_out[:, c], rows, i), ALU.add).then_inc(s_out[c], 1)

            def step(c, k, i):
                if k + 1 < NBLK:
                    split_low(c, k + 1, *share(k, i), i + BLOCKS[k][0] + 2)
                    new_rows(c, k, i)
                add_x(c, k, i)

            def group_rstd(c):
                pool.wait_ge(s_var, c + 1)
                nc.gpsimd.tensor_tensor(dev[:, c, 5, :], dev[:, c, 3, :], half[:], ALU.pow).then_inc(s_rstd, 1)

            for r, pairs in enumerate(ROUNDS):
                for c, k in pairs:
                    if k == 0:
                        group_rstd(c)
                        split_low(c, 0, 0, B, 1)
                run_round(pool, r, step)

        @block.tensor
        def _(pe):
            pe.wait_ge(s_consts, 32)
            pe.wait_ge(s_wsplit, 1)
            n = 0
            for l in range(2):
                for g in range(G):
                    for s in range(3):
                        dst = banks[0][n // 8][:].bitcast(F16)[:, (n % 8) * C:(n % 8 + 1) * C]
                        last = nc.tensor.transpose(dst, w_split[:, l, g, s, :], ident[:])
                        n += 1
            last.then_inc(s_wtrans, 1)
            def group_moments(c):
                for v, col in ((0, 0), (1, 16)):
                    pe.wait_ge(s_gm_in, 2 * c + v + 1)
                    nc.tensor.matmul(banks[c][3][:, col:col + B], gmean[:], dev[:, c, v, :],
                                     start=True, stop=True).then_inc(s_gm_out, 1)

            IS, SHIFT, OWN = 0, 1, 2

            def input_products(c, k, i):
                t0, n, lo, rows = BLOCKS[k]
                cols = B * rows
                hi = step_cols(x_hi[:, c, k % HBUF], rows, i)
                low = step_cols(x_lo[:, c, k % HBUF], rows, i)
                for g in range(G):
                    dst = banks[c][g][:, 0:cols]
                    nc.tensor.matmul(dst, w_t[:, 0, g, IS, :], hi, start=True, stop=False)
                    nc.tensor.matmul(dst, w_t[:, 1, g, IS, :], hi, start=False, stop=False)
                    nc.tensor.matmul(dst, w_t[:, 0, g, IS, :], low, start=False, stop=False)

            def state_products(c, k, h_low):
                t0, n, lo, rows = BLOCKS[k]
                cols = B * rows
                views = {}
                for part, first in ((SHIFT, lo), (OWN, lo + 1)):
                    views[part] = (h_hi[:, c, :, first:first + rows], h_lo[:, c, :, first:first + rows])
                out = [banks[c][g][:, 0:cols].rearrange("p (b r) -> p b r", b=B) for g in range(G)]

                def high(g):
                    for part in (SHIFT, OWN):
                        for l in range(2):
                            nc.tensor.matmul(out[g], w_t[:, l, g, part, :], views[part][0], start=False, stop=False)

                def low(g):
                    nc.tensor.matmul(out[g], w_t[:, 0, g, SHIFT, :], views[SHIFT][1], start=False, stop=False)
                    nc.tensor.matmul(out[g], w_t[:, 0, g, OWN, :], views[OWN][1],
                                     start=False, stop=True).then_inc(s_pre[c][g], 1)

                high(0)
                high(1)
                if h_low is not None:
                    pe.wait_ge(s_hlo[c], h_low)
                low(0)
                low(1)
                for g in (2, 3):
                    high(g)
                    low(g)

            def step(c, k, i):
                if not isinstance(i, int) or i == 0:
                    enter(c, k)
                if k == 0 and i == 0:
                    input_products(c, k, 0)
                    state_products(c, k, None)
                    return
                t = i + BLOCKS[k][0]
                pe.wait_ge(s_act[c][3], t)
                input_products(c, k, i)
                pe.wait_ge(s_hhi[c], t)
                state_products(c, k, t)

            def enter(c, k):
                t0, n, lo, rows = BLOCKS[k]
                pe.wait_ge(s_xlo[c], 1 + t0)
                if brings_rows(k):
                    pe.wait_ge(s_new[c], t0)

            for r, pairs in enumerate(ROUNDS):
                for c, k in pairs:
                    if k == 0:
                        group_moments(c)
                        if c == 0:
                            pe.wait_ge(s_wready, 1)
                            pe.wait_ge(s_init, 1)
                        pe.wait_ge(s_var, c + 1)
                run_round(pe, r, step)


def _diagonal_index():
    import numpy as np
    image, row, col = [], [], []
    for t0, n, lo, rows in BLOCKS:
        t, b, r = np.meshgrid(np.arange(t0, t0 + n), np.arange(B), np.arange(lo, lo + rows), indexing="ij")
        image.append(b.ravel())
        row.append(r.ravel())
        col.append((t - r).ravel())
    image, row, col = (np.concatenate(a) for a in (image, row, col))
    return image, row, col, (col >= 0) & (col < W)


def kernel(x, L0_conv_w_is, L0_conv_b_is, L0_conv_w_ss, L0_conv_b_ss):
    import numpy as np
    import concourse.bacc as bacc
    from concourse.bass_utils import run_bass_kernel_spmd

    x = np.asarray(x)
    w_is, b_is, w_ss, b_ss = (np.asarray(a) for a in (L0_conv_w_is, L0_conv_b_is, L0_conv_w_ss, L0_conv_b_ss))
    order = [1, 2, 3, 0]
    parts = np.stack([w_is, w_ss[:, :, 0], w_ss[:, :, 1]], axis=1)
    w_all = parts.reshape(G, C, 3, C)[order].transpose(1, 0, 2, 3)

    image, row, col, pixel = _diagonal_index()
    chains = x.reshape(CH, B, C, H, W)
    x_diag = np.zeros((CH, C, TOTAL), x.dtype)
    for c in range(CH):
        x_diag[c][:, pixel] = chains[c][image[pixel], :, row[pixel], col[pixel]].T

    arrays = {
        "x": np.ascontiguousarray(x.reshape(NB, C, H * W)),
        "x_diag": x_diag,
        "w_all": np.ascontiguousarray(w_all),
        "b_is": np.ascontiguousarray(b_is.reshape(G, C)[order].T),
        "b_ss": np.ascontiguousarray(b_ss.reshape(G, C)[order].T),
        "ident16": np.eye(P, dtype=np.float16),
        "group_mean": np.kron(np.eye(C // GROUP), np.full((GROUP, GROUP), 1.0 / GROUP)).astype(np.float32),
    }
    nc = bacc.Bacc("TRN2", target_bir_lowering=False, num_devices=1)
    args = [nc.dram_tensor(f"in_{n}", a.shape, mybir.dt.from_np(a.dtype), kind="ExternalInput").ap()
            for n, a in arrays.items()]
    args.append(nc.dram_tensor("out_diag", (CH, C, TOTAL), F32, kind="ExternalOutput").ap())
    diagonal_lstm_program(nc, *args)
    result = run_bass_kernel_spmd(nc, [{f"in_{n}": a for n, a in arrays.items()}], core_ids=[0])
    got = result.results[0]["out_diag"]
    out = np.empty((CH, B, C, H, W), got.dtype)
    for c in range(CH):
        out[c][image[pixel], :, row[pixel], col[pixel]] = got[c][:, pixel].T
    return out.reshape(NB, C, H, W)
```

```python
from contextlib import ExitStack

import concourse.bass as bass
from concourse import mybir

P = 128
C = 128
H = W = 64
NB = 16
CH = 2
B = NB // CH
G = 4
Q = 4
STEPS = H + W - 1
GROUP = 4
GN_EPS = 1e-5
SUB = 512
LATE = 3
PIECES = 4
NARROW = 16
LATER = 100
STAGES = 3
XBUF = 3
HBUF = 2

F32 = mybir.dt.float32
F16 = mybir.dt.float16
I32 = mybir.dt.int32
ALU = mybir.AluOpType
ACT = mybir.ActivationFunctionType
AX_X = mybir.AxisListType.X


def plan_blocks():
    blocks, t = [], 0
    while t < STEPS:
        n = Q if t else Q - 1
        lo = max(0, t - (W - 1))
        hi = min(t + n, H - 1)
        blocks.append((t, n, lo, hi - lo + 1))
        t += n
    return blocks


BLOCKS = plan_blocks()
NBLK = len(BLOCKS)
CHUNKS = H * W // SUB


def diagonal(t):
    lo = max(0, t - (W - 1))
    return lo * B, (min(t, H - 1) + 1 - lo) * B + left_column(t)


def left_column(t):
    return int(t < H - 1)


def entering(t):
    return sum(diagonal(t + 1)) - sum(diagonal(t)) if left_column(t) else 0


def tanh_later(c, t):
    return 0 < t and (c, t) != (CH - 1, STEPS - 1) and diagonal(t)[1] <= LATER


def run(start, step):
    for k, (_, n, _, _) in enumerate(BLOCKS):
        for i in range(n):
            for c in range(CH):
                if k == 0 and i == 0:
                    start(c)
                step(c, k, i)


def has_left(k):
    return left_column(BLOCKS[k][0] + BLOCKS[k][1] - 1) == 1


def share(k, i):
    each = -(-B // (BLOCKS[k][1] - 1))
    first = min(i * each, B)
    return first, min(each, B - first)


def prepares(k, i):
    return k + 1 < NBLK and i < BLOCKS[k][1] - 1


def normalised_last(c, k, i):
    other, j = (0, i) if c else (1, i - 1)
    return [(other, j)] if j >= 0 and prepares(k, j) else []


def shares_done(k, i):
    return 1 + sum(BLOCKS[j][1] - 1 for j in range(k)) + min(i + 1, BLOCKS[k][1] - 1)


def shares_of(k):
    return shares_done(k - 1, BLOCKS[k - 1][1]) if k else 1


OFFSET = [0]
for _t, _n, _lo, _rows in BLOCKS:
    OFFSET.append(OFFSET[-1] + _n * B * _rows)
TOTAL = OFFSET[-1]
MAXBLK = Q * B * H


def diagonal_lstm_program(nc, x, x_diag, w_all, b_is, b_ss, ident16, group_mean, out_diag):
    with ExitStack() as ctx:
        def sb(name, shape, dt):
            return ctx.enter_context(nc.sbuf_tensor(name, shape, dt))

        def sem(name):
            return ctx.enter_context(nc.semaphore(name))

        banks = [[ctx.enter_context(nc.psum_tensor(f"gate_{c}_{g}", [P, 512], F32)) for g in range(G)]
                 for c in range(CH)]
        w_nat = sb("w_nat", [P, G, 3, C], F32)
        w_split = sb("w_split", [P, 2, G, 3, C], F16)
        w_t = sb("w_t", [P, 2, G, 3, C], F16)
        ident = sb("ident", [P, P], F16)
        gmean = sb("gmean", [P, P], F32)
        bias_in = sb("bias_in", [P, 2, G], F32)
        bias = sb("bias", [P, G], F32)
        row_max = sb("row_max", [P, G], F32)
        row_exp = sb("row_exp", [P, G], I32)
        up = sb("up", [P, G], F32)
        down = sb("down", [P, G], F32)
        stage = sb("stage", [P, STAGES, H * W], F32)
        stats = sb("stats", [P, 2, CHUNKS, 6], F32)
        half = sb("half", [P, B], F32)
        moments = sb("moments", [P, NB, 2], F32)
        dev = sb("dev", [P, 4, NB], F32)
        mean = sb("mean", [P, NB], F32)
        rstd = sb("rstd", [P, NB], F32)
        x_raw = sb("x_raw", [P, CH, XBUF, MAXBLK], F32)
        x_norm = sb("x_norm", [P, CH, MAXBLK], F32)
        x_hi = sb("x_hi", [P, CH, HBUF, MAXBLK], F16)
        x_lo = sb("x_lo", [P, CH, HBUF, MAXBLK], F16)
        h_hi = sb("h_hi", [P, CH, (H + 1) * B], F16)
        h_lo = sb("h_lo", [P, CH, (H + 1) * B], F16)
        cell = sb("cell", [P, CH, H * B], F32)
        h_out = sb("h_out", [P, CH, MAXBLK], F32)
        act_f = sb("act_f", [P, CH, B * H], F32)
        act_i = sb("act_i", [P, CH, B * H], F32)
        act_g = sb("act_g", [P, CH, B * H], F32)
        act_o = sb("act_o", [P, CH, B * H], F32)
        tanh_c = act_i

        s_consts = sem("consts_loaded")
        s_weights = sem("weights_loaded")
        s_stage = [[sem(f"stage_loaded_{j}_{part}") for part in range(PIECES)] for j in range(STAGES)]
        s_stage_read = sem("stage_chunks_read")
        s_setup = sem("vector_setup_done")
        s_scales = sem("weight_scales_ready")
        s_whi = sem("weights_high_ready")
        s_wsplit = sem("weights_split")
        s_wtrans = sem("weights_transposed")
        s_wready = sem("weights_ready")
        s_moments = sem("moments_of_image_ready")
        s_gm_in = sem("second_moments_ready")
        s_gm_out = sem("group_moments_ready")
        s_var = sem("variance_ready")
        s_rstd = sem("rstd_ready")
        s_init = sem("state_zeroed")
        s_x = [[sem(f"x_loaded_{c}_{j}") for j in range(XBUF)] for c in range(CH)]
        s_store = [[sem(f"out_stored_{c}_{j}") for j in range(XBUF)] for c in range(CH)]
        s_centred = [sem(f"x_centred_{c}") for c in range(CH)]
        s_norm = [sem(f"x_normalised_{c}") for c in range(CH)]
        s_xhi = [sem(f"x_hi_ready_{c}") for c in range(CH)]
        s_xlo = [sem(f"x_lo_ready_{c}") for c in range(CH)]
        s_left = [sem(f"x_left_cleared_{c}") for c in range(CH)]
        s_pre = [[sem(f"gate_sum_{g}_{c}") for g in "figo"] for c in range(CH)]
        s_act = [[sem(f"gate_{g}_{c}") for g in "figo"] for c in range(CH)]
        s_fc = [sem(f"fc_ig_{c}") for c in range(CH)]
        s_c = [sem(f"cell_ready_{c}") for c in range(CH)]
        s_tc = [sem(f"tanh_cell_{c}") for c in range(CH)]
        s_h = [sem(f"h_ready_{c}") for c in range(CH)]
        s_hhi = [sem(f"h_hi_ready_{c}") for c in range(CH)]
        s_hlo = [sem(f"h_lo_ready_{c}") for c in range(CH)]
        s_new = [sem(f"new_cells_set_{c}") for c in range(CH)]
        s_out = [sem(f"out_added_{c}") for c in range(CH)]

        def block_ap(buf, k):
            _, n, _, rows = BLOCKS[k]
            return buf[:, 0:n * rows * B].rearrange("p (s r b) -> p s r b", s=n, b=B)

        def step_columns(buf, k, i):
            t0, _, first, rows = BLOCKS[k]
            lo, n = diagonal(t0 + i)
            start = i * rows * B + lo - first * B
            return buf[:, start:start + n]

        block = ctx.enter_context(nc.Block())

        @block.sync
        def _(sp):
            def load_image(m):
                if m >= STAGES:
                    sp.wait_ge(s_stage_read, CHUNKS * (m - STAGES + 1))
                for part in range(PIECES):
                    cols = slice(part * (H * W // PIECES), (part + 1) * (H * W // PIECES))
                    sp.dma_start(stage[:, m % STAGES, cols], x[m, :, cols]).then_inc(s_stage[m % STAGES][part], 16)

            def load(c, k):
                n = OFFSET[k + 1] - OFFSET[k]
                j = k % XBUF
                if k >= XBUF:
                    sp.wait_ge(s_store[c][j], 16 * (k // XBUF))
                sp.dma_start(x_raw[:, c, j, 0:n], x_diag[c, :, OFFSET[k]:OFFSET[k + 1]]).then_inc(s_x[c][j], 16)

            def store(c, k):
                t0, n, _, _ = BLOCKS[k]
                sp.wait_ge(s_out[c], t0 + n)
                size = OFFSET[k + 1] - OFFSET[k]
                sp.dma_start(out_diag[c, :, OFFSET[k]:OFFSET[k + 1]],
                             x_raw[:, c, k % XBUF, 0:size]).then_inc(s_store[c][k % XBUF], 16)

            load_image(0)
            sp.dma_start(w_nat[:], w_all).then_inc(s_weights, 16)
            sp.dma_start(bias_in[:, 0, :], b_is).then_inc(s_weights, 16)
            sp.dma_start(bias_in[:, 1, :], b_ss).then_inc(s_weights, 16)
            sp.dma_start(ident[:], ident16).then_inc(s_consts, 16)
            sp.dma_start(gmean[:], group_mean).then_inc(s_consts, 16)
            for m in range(1, NB):
                load_image(m)
                if m == B:
                    load(0, 0)
                    load(0, 1)
                    load(1, 0)
            load(1, 1)
            for c in range(CH):
                for k in range(2, XBUF):
                    load(c, k)
            for k in range(1, NBLK):
                for c in range(CH):
                    store(c, k - 1)
                    if k + XBUF - 1 < NBLK:
                        load(c, k + XBUF - 1)
            for c in range(CH):
                store(c, NBLK - 1)
            for c in range(CH):
                for j in range(XBUF):
                    sp.wait_ge(s_store[c][j], 16 * len(range(j, NBLK, XBUF)))

        @block.vector
        def _(dve):
            done = [0]
            centred = [0] * CH

            def link(ins):
                done[0] += 1
                ins.then_inc(s_setup, 1)
                dve.wait_ge(s_setup, done[0])

            def chunk_stats(n):
                m, part = divmod(n, CHUNKS)
                piece = CHUNKS // PIECES
                if part % piece == 0:
                    dve.wait_ge(s_stage[m % STAGES][part // piece], 16 * (m // STAGES + 1))
                if part == 0 and m >= 2:
                    dve.wait_ge(s_moments, m - 1)
                nc.vector.bn_stats(stats[:, m % 2, part, :],
                                   stage[:, m % STAGES, part * SUB:(part + 1) * SUB]).then_inc(s_stage_read, 1)

            def image_moments(m):
                dve.wait_ge(s_stage_read, CHUNKS * (m + 1))
                nc.vector.bn_aggr(moments[:, m, :],
                                  stats[:, m % 2].rearrange("p n k -> p (n k)")).then_inc(s_moments, 1)

            def image_stats(first, end, done=0):
                for m in range(first, end):
                    for part in range(done if m == first else 0, CHUNKS):
                        chunk_stats(m * CHUNKS + part)
                        if part == 0 and m > first:
                            image_moments(m - 1)
                image_moments(end - 1)

            def group_stats(c):
                own = slice(c * B, (c + 1) * B)

                def meanwhile(n):
                    if c == 0:
                        for part in range(2 * n, 2 * n + 2):
                            chunk_stats(B * CHUNKS + part)

                second, variance, power, temp, centre, scale = (
                    buf[:, own] for buf in (dev[:, 0], dev[:, 1], dev[:, 2], dev[:, 3], mean, rstd))
                meanwhile(0)
                dve.wait_ge(s_gm_out, 2 * c + 1)
                nc.vector.tensor_copy(centre, banks[c][3][:, 0:B])
                link(nc.vector.tensor_tensor(second, moments[:, own, 0], banks[c][3][:, 0:B], ALU.subtract))
                link(nc.vector.tensor_tensor(second, second, second, ALU.mult))
                nc.vector.tensor_tensor(second, second, moments[:, own, 1], ALU.add).then_inc(s_gm_in, 1)
                meanwhile(1)
                dve.wait_ge(s_gm_out, 2 * c + 2)
                nc.vector.tensor_scalar(variance, banks[c][3][:, B:2 * B], GN_EPS, None, ALU.add).then_inc(s_var, 1)
                meanwhile(2)
                dve.wait_ge(s_rstd, c + 1)
                link(nc.vector.tensor_tensor(temp, power, power, ALU.mult))
                link(nc.vector.tensor_tensor(temp, temp, variance, ALU.mult))
                link(nc.vector.tensor_scalar(temp, temp, -0.5, 1.5, ALU.mult, ALU.add))
                link(nc.vector.tensor_tensor(scale, power, temp, ALU.mult))

            image_stats(0, 1)

            dve.wait_ge(s_weights, 48)
            nc.vector.tensor_tensor(bias[:], bias_in[:, 0, :], bias_in[:, 1, :], ALU.add)
            link(nc.vector.tensor_reduce(row_max[:], w_nat[:].rearrange("p g s i -> p g (s i)"), AX_X, ALU.max,
                                         apply_absolute_value=True))
            link(nc.vector.tensor_scalar(row_max[:], row_max[:], 2.0 ** -110, None, ALU.max))
            link(nc.vector.tensor_scalar(row_exp[:], row_max[:].bitcast(I32), 0x7F800000, None, ALU.bitwise_and))
            nc.vector.tensor_scalar(up[:].bitcast(I32), row_exp[:], -1.0, float(267 << 23), ALU.mult, ALU.add)
            nc.vector.tensor_scalar(down[:].bitcast(I32), row_exp[:], float(13 << 23), None,
                                    ALU.subtract).then_inc(s_scales, 1)

            def normalise(c, k, first, count):
                src = block_ap(x_raw[:, c, k % XBUF], k)
                dst = block_ap(x_norm[:, c], k)
                _, steps, _, rows = BLOCKS[k]
                if rows <= NARROW:
                    src, dst = (v[:, :, :, first:first + count] for v in (src, dst))
                    m = slice(c * B + first, c * B + first + count)
                    each = lambda v: v[:, m].unsqueeze(1).unsqueeze(1).to_broadcast([P, steps, rows, count])
                    nc.vector.tensor_tensor(dst, src, each(mean), ALU.subtract).then_inc(s_centred[c], 1)
                    centred[c] += 1
                    dve.wait_ge(s_centred[c], centred[c])
                    nc.vector.tensor_tensor(dst, dst, each(rstd), ALU.mult).then_inc(s_norm[c], 1)
                    return
                for b in range(first, first + count):
                    m = c * B + b
                    last = nc.vector.tensor_scalar(dst[:, :, :, b], src[:, :, :, b], mean[:, m:m + 1],
                                                   rstd[:, m:m + 1], ALU.subtract, ALU.mult)
                last.then_inc(s_norm[c], 1)

            def block_arrived(c, k):
                dve.wait_ge(s_x[c][k % XBUF], 16 * (k // XBUF + 1))
                if k > 0:
                    dve.wait_ge(s_xlo[c], shares_of(k - 1))

            def cell_update(c, t):
                lo, n = diagonal(t)
                own, state = slice(0, n), cell[:, c, lo:lo + n]
                if t > 0 and entering(t - 1):
                    dve.wait_ge(s_new[c], t)
                dve.wait_ge(s_act[c][0], t + 1)
                nc.vector.tensor_tensor(act_f[:, c, own], act_f[:, c, own], state, ALU.mult)
                dve.wait_ge(s_act[c][2], t + 1)
                nc.vector.tensor_tensor(act_g[:, c, own], act_g[:, c, own], act_i[:, c, own],
                                        ALU.mult).then_inc(s_fc[c], 1)
                dve.wait_ge(s_fc[c], t + 1)
                nc.vector.tensor_tensor(state, act_f[:, c, own], act_g[:, c, own], ALU.add).then_inc(s_c[c], 1)

            def hidden(c, k, i):
                t = BLOCKS[k][0] + i
                lo, n = diagonal(t)
                more = entering(t)
                end = lo + n
                own, left = slice(0, n), slice(n - 1, n)
                h = h_out[:, c, i * B * H:(i + 1) * B * H]
                o, tanh = act_o[:, c], tanh_c[:, c]
                hi, low = h_hi[:, c, B + lo:B + end], h_lo[:, c, B + lo:B + end]
                hi_left = h_hi[:, c, B + end - 1:B + end]
                spread = lambda column: column.to_broadcast([P, more])
                if k > 0:
                    dve.wait_ge(s_out[c], BLOCKS[k - 1][0] + min(i + 1, BLOCKS[k - 1][1]))
                dve.wait_ge(s_tc[c], t + 1)
                last = nc.vector.tensor_tensor(hi, o[:, own], tanh[:, own], ALU.mult)
                if more:
                    last = nc.vector.tensor_tensor(h_hi[:, c, B + end:B + end + more], spread(o[:, left]),
                                                   spread(tanh[:, left]), ALU.mult)
                last.then_inc(s_hhi[c], 1)
                nc.vector.tensor_tensor(h[:, own], o[:, own], tanh[:, own], ALU.mult).then_inc(s_h[c], 1)
                if more:
                    dve.wait_ge(s_c[c], t + 1)
                    nc.vector.tensor_scalar(cell[:, c, end:end + more], spread(cell[:, c, end - 1:end]), 1.0, None,
                                            ALU.mult).then_inc(s_new[c], 1)
                dve.wait_ge(s_h[c], t + 1)
                last = nc.vector.tensor_tensor(low, h[:, own], hi, ALU.subtract)
                if more:
                    last = nc.vector.tensor_tensor(h_lo[:, c, B + end:B + end + more], spread(h[:, left]),
                                                   spread(hi_left), ALU.subtract)
                last.then_inc(s_hlo[c], 1)

            def step(c, k, i):
                cell_update(c, BLOCKS[k][0] + i)
                if prepares(k, i):
                    if i == 0:
                        block_arrived(c, k + 1)
                    normalise(c, k + 1, *share(k, i))
                hidden(c, k, i)

            def start(c):
                if c == 0:
                    image_stats(1, B)
                else:
                    image_stats(NB - LATE, NB)
                group_stats(c)
                block_arrived(c, 0)
                normalise(c, 0, 0, B)
                if c == 0:
                    image_stats(B, NB - LATE, done=6)

            run(start, step)

        @block.scalar
        def _(act):
            def split_high(c, k, first, count, n):
                act.wait_ge(s_norm[c], n)
                images = slice(first, first + count)
                nc.scalar.copy(block_ap(x_hi[:, c, k % HBUF], k)[:, :, :, images],
                               block_ap(x_norm[:, c], k)[:, :, :, images]).then_inc(s_xhi[c], 1)

            def gate(c, t, g):
                n = diagonal(t)[1]
                buf, func = ((act_f, ACT.Sigmoid), (act_i, ACT.Sigmoid), (act_g, ACT.Tanh), (act_o, ACT.Sigmoid))[g]
                act.wait_ge(s_pre[c][g], t + 1)
                nc.scalar.activation(buf[:, c, 0:n], banks[c][g][:, 0:n], func, bias=bias[:, g:g + 1],
                                     scale=down[:, g:g + 1]).then_inc(s_act[c][g], 1)

            def tanh_cell(c, t):
                lo, n = diagonal(t)
                act.wait_ge(s_c[c], t + 1)
                nc.scalar.activation(tanh_c[:, c, 0:n], cell[:, c, lo:lo + n], ACT.Tanh).then_inc(s_tc[c], 1)

            def step(c, k, i):
                t0 = BLOCKS[k][0]
                gate(c, t0 + i, 0)
                before = (0, t0 + i) if c else (1, t0 + i - 1)
                if tanh_later(*before):
                    tanh_cell(*before)
                for g in range(1, G):
                    gate(c, t0 + i, g)
                for other, j in normalised_last(c, k, i):
                    if j == 0 and k > 0:
                        act.wait_ge(s_pre[other][3], t0)
                    split_high(other, k + 1, *share(k, j), shares_done(k, j))
                if not tanh_later(c, t0 + i):
                    tanh_cell(c, t0 + i)

            act.wait_ge(s_scales, 1)
            for g in range(G):
                nc.scalar.activation(w_split[:, 0, g], w_nat[:, g], ACT.Identity, scale=up[:, g:g + 1])
            for g in range(G):
                last = nc.scalar.activation(w_nat[:, g], w_nat[:, g], ACT.Identity, scale=up[:, g:g + 1])
            last.then_inc(s_whi, 1)
            wt = w_t[:].rearrange("p l g s i -> p (l g s i)")
            act.wait_ge(s_wtrans, 1)
            for n in range(3):
                last = nc.scalar.copy(wt[:, 1024 * n:1024 * n + 1024], banks[0][n][:].bitcast(F16))
            last.then_inc(s_wready, 1)
            run(lambda c: split_high(c, 0, 0, B, 1), step)

        @block.gpsimd
        def _(pool):
            def split_low(c, k, first, count, n):
                pool.wait_ge(s_xhi[c], n)
                images = slice(first, first + count)
                nc.gpsimd.tensor_tensor(block_ap(x_lo[:, c, k % HBUF], k)[:, :, :, images],
                                        block_ap(x_norm[:, c], k)[:, :, :, images],
                                        block_ap(x_hi[:, c, k % HBUF], k)[:, :, :, images],
                                        ALU.subtract).then_inc(s_xlo[c], 1)

            def clear_left(c, k, n):
                t0, steps, _, rows = BLOCKS[k]
                pool.wait_ge(s_xlo[c], n)
                for buf in (x_hi, x_lo):
                    last = nc.gpsimd.memset(buf[:, c, k % HBUF, bass.ds((t0 + 1) * B, steps, (rows + 1) * B)], 0.0)
                last.then_inc(s_left[c], 1)

            def add_x(c, k, i):
                t = BLOCKS[k][0] + i
                pool.wait_ge(s_h[c], t + 1)
                here = step_columns(x_raw[:, c, k % XBUF], k, i)
                h = h_out[:, c, i * B * H:i * B * H + diagonal(t)[1]]
                nc.gpsimd.tensor_tensor(here, here, h, ALU.add).then_inc(s_out[c], 1)

            def step(c, k, i):
                for other, j in normalised_last(c, k, i):
                    split_low(other, k + 1, *share(k, j), shares_done(k, j))
                    if not prepares(k, j + 1) and has_left(k + 1):
                        clear_left(other, k + 1, shares_done(k, j))
                add_x(c, k, i)

            def start(c):
                own = slice(c * B, (c + 1) * B)
                pool.wait_ge(s_var, c + 1)
                nc.gpsimd.tensor_tensor(dev[:, 2, own], dev[:, 1, own], half[:, 0:B], ALU.pow).then_inc(s_rstd, 1)
                split_low(c, 0, 0, B, 1)
                clear_left(c, 0, 1)

            nc.gpsimd.memset(half[:], -0.5)
            nc.gpsimd.memset(h_hi[:], 0.0)
            nc.gpsimd.memset(h_lo[:], 0.0)
            nc.gpsimd.memset(cell[:], 0.0).then_inc(s_init, 1)
            pool.wait_ge(s_whi, 1)
            nc.gpsimd.tensor_tensor(w_split[:, 1].rearrange("p g s i -> p (g s i)"),
                                    w_nat[:].rearrange("p g s i -> p (g s i)"),
                                    w_split[:, 0].rearrange("p g s i -> p (g s i)"), ALU.subtract).then_inc(s_wsplit, 1)
            run(start, step)

        @block.tensor
        def _(pe):
            pe.wait_ge(s_consts, 32)
            pe.wait_ge(s_wsplit, 1)
            n = 0
            for l in range(2):
                for g in range(G):
                    for s in range(3):
                        dst = banks[0][n // 8][:].bitcast(F16)[:, (n % 8) * C:(n % 8 + 1) * C]
                        last = nc.tensor.transpose(dst, w_split[:, l, g, s, :], ident[:])
                        n += 1
            last.then_inc(s_wtrans, 1)

            def start(c):
                if c == 0:
                    pe.wait_ge(s_init, 1)
                    pe.wait_ge(s_wready, 1)
                pe.wait_ge(s_moments, (c + 1) * B)
                nc.tensor.matmul(banks[c][3][:, 0:B], gmean[:], moments[:, c * B:(c + 1) * B, 0],
                                 start=True, stop=True).then_inc(s_gm_out, 1)
                pe.wait_ge(s_gm_in, c + 1)
                nc.tensor.matmul(banks[c][3][:, B:2 * B], gmean[:], dev[:, 0, c * B:(c + 1) * B],
                                 start=True, stop=True).then_inc(s_gm_out, 1)
                pe.wait_ge(s_var, c + 1)

            IS, SHIFT, OWN = 0, 1, 2

            def input_products(c, k, i):
                n = diagonal(BLOCKS[k][0] + i)[1]
                hi = step_columns(x_hi[:, c, k % HBUF], k, i)
                low = step_columns(x_lo[:, c, k % HBUF], k, i)
                for g in range(G):
                    out = banks[c][g][:, 0:n]
                    nc.tensor.matmul(out, w_t[:, 0, g, IS, :], hi, start=True, stop=False)
                    nc.tensor.matmul(out, w_t[:, 1, g, IS, :], hi, start=False, stop=False)
                    nc.tensor.matmul(out, w_t[:, 0, g, IS, :], low, start=False, stop=False)

            def state_products(c, t):
                lo, n = diagonal(t)
                high_of, low_of = ({part: buf[:, c, first:first + n] for part, first in ((SHIFT, lo), (OWN, lo + B))}
                                   for buf in (h_hi, h_lo))
                out = [banks[c][g][:, 0:n] for g in range(G)]

                def high(g):
                    for part in (SHIFT, OWN):
                        for l in range(2):
                            nc.tensor.matmul(out[g], w_t[:, l, g, part, :], high_of[part], start=False, stop=False)

                def low(g):
                    nc.tensor.matmul(out[g], w_t[:, 0, g, SHIFT, :], low_of[SHIFT], start=False, stop=False)
                    nc.tensor.matmul(out[g], w_t[:, 0, g, OWN, :], low_of[OWN],
                                     start=False, stop=True).then_inc(s_pre[c][g], 1)

                if t > 0:
                    pe.wait_ge(s_hhi[c], t)
                high(0)
                high(1)
                if t > 0:
                    pe.wait_ge(s_hlo[c], t)
                low(0)
                low(1)
                for g in (2, 3):
                    high(g)
                    low(g)

            def step(c, k, i):
                t = BLOCKS[k][0] + i
                if i == 0 and has_left(k):
                    pe.wait_ge(s_left[c], k + 1)
                elif i == 0:
                    pe.wait_ge(s_xlo[c], shares_of(k))
                if t > 0:
                    pe.wait_ge(s_act[c][3], t)
                input_products(c, k, i)
                state_products(c, t)

            run(start, step)


def _diagonal_index():
    import numpy as np
    image, row, col = [], [], []
    for t0, n, lo, rows in BLOCKS:
        t, r, b = np.meshgrid(np.arange(t0, t0 + n), np.arange(lo, lo + rows), np.arange(B), indexing="ij")
        image.append(b.ravel())
        row.append(r.ravel())
        col.append((t - r).ravel())
    image, row, col = (np.concatenate(a) for a in (image, row, col))
    return image, row, col, (col >= 0) & (col < W)


def kernel(x, L0_conv_w_is, L0_conv_b_is, L0_conv_w_ss, L0_conv_b_ss):
    import numpy as np
    import concourse.bacc as bacc
    from concourse.bass_utils import run_bass_kernel_spmd

    x = np.asarray(x)
    w_is, b_is, w_ss, b_ss = (np.asarray(a) for a in (L0_conv_w_is, L0_conv_b_is, L0_conv_w_ss, L0_conv_b_ss))
    order = [1, 2, 3, 0]
    parts = np.stack([w_is, w_ss[:, :, 0], w_ss[:, :, 1]], axis=1)
    w_all = parts.reshape(G, C, 3, C)[order].transpose(1, 0, 2, 3)

    image, row, col, pixel = _diagonal_index()
    chains = x.reshape(CH, B, C, H, W)
    x_diag = np.zeros((CH, C, TOTAL), x.dtype)
    for c in range(CH):
        x_diag[c][:, pixel] = chains[c][image[pixel], :, row[pixel], col[pixel]].T

    arrays = {
        "x": np.ascontiguousarray(x.reshape(NB, C, H * W)),
        "x_diag": x_diag,
        "w_all": np.ascontiguousarray(w_all),
        "b_is": np.ascontiguousarray(b_is.reshape(G, C)[order].T),
        "b_ss": np.ascontiguousarray(b_ss.reshape(G, C)[order].T),
        "ident16": np.eye(P, dtype=np.float16),
        "group_mean": np.kron(np.eye(C // GROUP), np.full((GROUP, GROUP), 1.0 / GROUP)).astype(np.float32),
    }
    nc = bacc.Bacc("TRN2", target_bir_lowering=False, num_devices=1)
    args = [nc.dram_tensor(f"in_{n}", a.shape, mybir.dt.from_np(a.dtype), kind="ExternalInput").ap()
            for n, a in arrays.items()]
    args.append(nc.dram_tensor("out_diag", (CH, C, TOTAL), F32, kind="ExternalOutput").ap())
    diagonal_lstm_program(nc, *args)
    result = run_bass_kernel_spmd(nc, [{f"in_{n}": a for n, a in arrays.items()}], core_ids=[0])
    got = result.results[0]["out_diag"]
    out = np.empty((CH, B, C, H, W), got.dtype)
    for c in range(CH):
        out[c][image[pixel], :, row[pixel], col[pixel]] = got[c][:, pixel].T
    return out.reshape(NB, C, H, W)
```
